# Optimizing a Trainium2 kernel written in Bass

```python
import numpy as np
import jax
import jax.numpy as jnp

def _softmax(x, axis=-1):
    return jax.nn.softmax(x, axis=axis)

def _gelu(x):
    return jax.nn.gelu(x, approximate=True)

def _silu(x):
    return jax.nn.silu(x)

def _sigmoid(x):
    return jax.nn.sigmoid(x)

def _layernorm(x, axis=-1, eps=1e-05):
    m = jnp.mean(x, axis=axis, keepdims=True)
    v = jnp.var(x, axis=axis, keepdims=True)
    return (x - m) / jnp.sqrt(v + eps)

def _scatter_add(tgt, idx, src, axis=0):
    return tgt.at[idx].add(src)

def _segment_sum(src, seg, n):
    return jax.ops.segment_sum(src, seg, n)
kernel_name = 'mk_cond_resid_d1_seqx_r4_167498'

def setup_inputs(seed: int=0):
    np.random.seed(seed)
    _w = jnp.asarray

    def _rec_inputs():
        import jax
        import jax.numpy as jnp
        _rk = jax.random.key(seed)
        x = -0.000125 + 0.9999 * jax.random.normal(jax.random.fold_in(_rk, 1), (128, 64, 1024), jnp.float32)
        _lenS = 64 - jax.random.randint(jax.random.fold_in(_rk, 7), (128,), 0, max(1, 64 // 4) + 1, jnp.int32)
        _lenS2 = 64 - jax.random.randint(jax.random.fold_in(_rk, 8), (128,), 0, max(1, 64 // 4) + 1, jnp.int32)
        condB_codebook = -0.0625 + 0.715345 * jax.random.normal(jax.random.fold_in(_rk, 11), (128,), jnp.float32)
        return (x, condB_codebook)
    x, condB_codebook = _rec_inputs()

    def _L0_cond_setup():
        import jax, jax.numpy as jnp
        import numpy as np
        GROUP = 128
        LORA_ALPHA = 32.0
        LORA_RANK = 64
        key = jax.random.key(seed)
        k1, k2, k3, k4 = jax.random.split(key, 4)
        O, I = (1024, 1024)
        x = jax.random.normal(k1, (4, 512, I), dtype=jnp.float32)
        weight = jax.random.normal(k2, (O, I), dtype=jnp.float32) * 0.02
        wg = weight.reshape(O, I // GROUP, GROUP)
        scale_log = jnp.log(jnp.clip(jnp.max(jnp.abs(wg), axis=2, keepdims=True), 1e-05))
        codebook = jnp.array([-1.0, -0.25, 0.0, 1.0], dtype=jnp.float32)
        lora_A = jax.random.normal(k3, (LORA_RANK, I), dtype=jnp.float32) * 0.02
        lora_B = jax.random.normal(k4, (O, LORA_RANK), dtype=jnp.float32) * 0.02
        return {'x': x, 'weight': weight, 'scale_log': scale_log, 'codebook': codebook, 'lora_A': lora_A, 'lora_B': lora_B}
    _L0_cond_all = _L0_cond_setup()
    _L0_cond_in = {k: v for k, v in _L0_cond_all.items() if k in ('weight', 'scale_log', 'lora_A', 'lora_B')}
    del _L0_cond_all
    return {'x': x, 'condB_codebook': condB_codebook, 'L0_cond_weight': _L0_cond_in['weight'], 'L0_cond_scale_log': _L0_cond_in['scale_log'], 'L0_cond_lora_A': _L0_cond_in['lora_A'], 'L0_cond_lora_B': _L0_cond_in['lora_B']}

def reference(x, condB_codebook, L0_cond_weight, L0_cond_scale_log, L0_cond_lora_A, L0_cond_lora_B):
    import jax
    import jax.numpy as jnp

    def _L0_cond_ref(x, weight, scale_log, codebook, lora_A, lora_B):
        import jax, jax.numpy as jnp
        import numpy as np
        GROUP = 128
        LORA_ALPHA = 32.0
        LORA_RANK = 64
        O, I = weight.shape
        lora_delta = lora_B @ lora_A * (LORA_ALPHA / LORA_RANK)
        cb = codebook / jnp.clip(jnp.max(jnp.abs(codebook)), 1e-08)
        scale = jnp.exp(scale_log)
        wg = (weight + lora_delta).reshape(O, I // GROUP, GROUP)
        normalized = wg / scale
        thresholds = (cb[:-1] + cb[1:]) * 0.5
        idx = jnp.searchsorted(thresholds, normalized, side='left')
        quantized = cb[idx]
        w = jax.lax.stop_gradient(quantized - normalized) + normalized
        w_q = (w * scale).reshape(O, I)
        w_eff = w_q + lora_delta
        return x @ w_eff.T
    x = x + _L0_cond_ref(x, L0_cond_weight, L0_cond_scale_log, condB_codebook, L0_cond_lora_A, L0_cond_lora_B)
    return x

_drawn_inputs = setup_inputs


def setup_inputs(seed=0):
    import zlib

    import numpy as np

    out = dict(_drawn_inputs(seed))
    spreads = {}
    factors = {}
    for name, (base, spread) in spreads.items():
        noise = np.random.default_rng([zlib.crc32(name.encode()), seed]).standard_normal(out[name].shape)
        drawn = base * np.exp(spread * noise) if base else spread * noise
        out[name] = jnp.asarray(drawn.astype(out[name].dtype))
    for name, factor in factors.items():
        out[name] = (out[name] * factor).astype(out[name].dtype)
    return out
```

```python
from contextlib import ExitStack

import concourse.bass as bass
from concourse import mybir

P = 128
ALU = mybir.AluOpType
ACT = mybir.ActivationFunctionType
AX = mybir.AxisListType
F32 = mybir.dt.float32
F32R = mybir.dt.float32r
I32 = mybir.dt.int32
U32 = mybir.dt.uint32

ROUND = 12582912.0
LOG2E = 1.4426950408889634
LN2_HI = 0.693145751953125
LN2_LO = 1.428606765330187e-06
NEVER = 3.0e38
LORA_SCALE = 32.0 / 64.0
MAX_PIECES = 128


def cond_residual_kernel(nc, x, codebook, weight, scale_log, lora_a, lora_b, out):
    I = x.shape[-1]
    O = weight.shape[0]
    ROWS = x.shape[0] * x.shape[1]
    RANK = lora_a.shape[0]
    NCB = codebook.shape[0]
    GROUPS = scale_log.shape[1]
    GSIZE = I // GROUPS
    C = I // P
    Q = P // 32
    KQ = I // Q
    OT = O // P
    TILES = ROWS // P
    GR = 2 * P
    NG = ROWS // GR
    RES = 4
    RT = RES * GR // P
    OB = 2 * P
    NB = O // OB
    H = 512
    LEVELS = NCB.bit_length() - 1
    assert 1 << LEVELS == NCB == P and I == O and NG % RES == 0

    xg = x.rearrange("s l k -> (s l) k").rearrange("(g b j) (a k) -> g a j b k", b=GR // 32, j=32, a=Q)
    og = out.rearrange("s l o -> (s l) o").rearrange("(t p) o -> t p o", p=P)
    wt = weight.rearrange("(t p) k -> t p k", p=P)
    sl = scale_log.rearrange("(t p) g one -> p t (g one)", p=P)
    lb = lora_b.rearrange("(t p) r -> p t r", p=P)
    cb_rows = codebook.partition_broadcast(P)

    with ExitStack() as ctx:
        def sb(name, shape, dt=F32):
            return ctx.enter_context(nc.sbuf_tensor(name, shape, dt))

        def ps(name, shape):
            return ctx.enter_context(nc.psum_tensor(name, shape, F32))

        def sem(name):
            return ctx.enter_context(nc.semaphore(name))

        w_hi = sb("w_hi", [P, C, O], F32R)
        w_lo = sb("w_lo", [P, C, O], F32R)
        x_hi = sb("x_hi", [P, RES, C, GR], F32R)
        x_lo = sb("x_lo", [P, RES, C, GR], F32R)
        x_raw = sb("x_raw", [P, 2, GR // 32, KQ])
        x_t = sb("x_t", [P, C, GR])
        y_out = sb("y_out", [P, 2, O])
        w_raw = sb("w_raw", [P, 2, I])
        w_q = sb("w_q", [P, I])
        w_eff = sb("w_eff", [P, C, Q, 32])
        mask = sb("mask", [P, I], U32)
        delta = sb("delta", [P, 2, I])
        a_sb = sb("a_sb", [RANK, I])
        b_sb = sb("b_sb", [P, OT, RANK])
        b_t = sb("b_t", [RANK, O])
        ident = sb("ident", [P, P])
        ones = sb("ones", [P, P])
        s_log = sb("s_log", [P, OT * GROUPS])
        s_k = sb("s_k", [P, OT * GROUPS])
        s_k1 = sb("s_k1", [P, OT * GROUPS])
        s_p1 = sb("s_p1", [P, OT * GROUPS], I32)
        s_p2 = sb("s_p2", [P, OT * GROUPS], I32)
        s_e = sb("s_e", [P, OT * GROUPS])
        scale = sb("scale", [P, OT * GROUPS])
        s_inv = sb("s_inv", [P, OT * GROUPS])
        cb = sb("cb", [P, NCB])
        cb_max = sb("cb_max", [P, 2])
        thr = sb("thr", [P, NCB])
        lower = sb("lower", [P, NCB])
        upper = sb("upper", [P, NCB])
        alive = sb("alive", [P, NCB])
        zeros = sb("zeros", [P, NCB])
        count = sb("count", [P, NCB])
        junk = sb("junk", [P, 2, NCB])
        number = sb("number", [P, 1])
        column = sb("column", [P, 3])
        diag = sb("diag", [P, 2, NCB])
        pieces = sb("pieces", [P, 2, NCB])
        value = sb("value", [P, 1])
        trips = sb("trips", [P, 1], I32)

        acc = ps("acc", [P, 4, H])
        p_delta = ps("p_delta", [P, I])
        p_turn = ps("p_turn", [P, C, P])

        x_in = [sem(f"x_in{i}") for i in range(2)]
        w_in = [sem(f"w_in{i}") for i in range(2)]
        y_gone = [sem(f"y_gone{i}") for i in range(2)]
        cb_in = sem("cb_in")
        sl_in = sem("sl_in")
        a_in = sem("a_in")
        b_in = sem("b_in")
        consts_set = sem("consts_set")
        number_set = sem("number_set")
        step = sem("step")
        b_turned = sem("b_turned")
        bt_ready = sem("bt_ready")
        diag_ready = sem("diag_ready")
        lists_made = sem("lists_made")
        delta_made = sem("delta_made")
        delta_copied = sem("delta_copied")
        delta_added = sem("delta_added")
        piece_done = sem("piece_done")
        wq_diff = sem("wq_diff")
        weff_made = sem("weff_made")
        pool_step = sem("pool_step")
        w_turned = sem("w_turned")
        whi_ready = sem("whi_ready")
        wlo_ready = sem("wlo_ready")
        xt_ready = sem("xt_ready")
        xhi_ready = sem("xhi_ready")
        xlo_ready = sem("xlo_ready")
        sums_done = sem("sums_done")
        y_ready = sem("y_ready")

        UNITS = NB * RT
        LATE = TILES - RT

        block = ctx.enter_context(nc.Block())

        def acc_unit(u):
            return acc[:, u % 4, 0:OB]

        @block.sync
        def _(sp):
            def load_x(g, slot):
                for a in range(Q):
                    src = xg[g, a] if isinstance(g, int) else xg[bass.ds(g, 1), a].rearrange("g j b k -> (g j) b k")
                    sp.dma_start(x_raw[32 * a:32 * a + 32, slot], src).then_inc(x_in[slot], 16)

            sp.dma_start(w_raw[:, 0], wt[0]).then_inc(w_in[0], 16)
            load_x(0, 0)
            sp.dma_start(w_raw[:, 1], wt[1]).then_inc(w_in[1], 16)
            load_x(1, 1)

            def store_unit(u):
                sp.wait_ge(y_ready, u + 1)
                t, b = u % RT, u // RT
                sp.dma_start(og[t][:, b * OB:(b + 1) * OB], y_out[:, u % 2, 0:OB]).then_inc(y_gone[u % 2], 16)

            for g in range(2, RES):
                sp.wait_ge(xt_ready, g - 1)
                load_x(g, g % 2)
            for u in range(2):
                store_unit(u)
            for g in range(RES, RES + 2):
                sp.wait_ge(xt_ready, g - 1)
                load_x(g, g % 2)
            for u in range(2, UNITS):
                store_unit(u)

            def turn(n, last):
                for r in range(RES):
                    if not (last and r >= RES - 2):
                        sp.wait_ge(xt_ready, (n + 1) * RES + r + 1)
                        load_x((n + 1) * RES + r + 2, r % 2)
                    for h in range(2):
                        t = 2 * r + h
                        sp.wait_ge(y_ready, UNITS + n * RT + t + 1)
                        dst = og[(n + 1) * RT + t] if isinstance(n, int) else og[bass.ds((n + 1) * RT + t, 1)].rearrange("t p o -> (t p) o")
                        sp.dma_start(dst, y_out[:, t % 2]).then_inc(y_gone[t % 2], 16)

            turns = NG // RES - 1
            with sp.Fori(0, turns - 1) as n:
                turn(n, False)
            turn(turns - 1, True)
            for i in range(2):
                sp.wait_ge(y_gone[i], 16 * (UNITS + LATE) // 2)

        @block.gpsimd
        def _(pool):
            pool.memset(ident[:], 0.0).then_inc(pool_step, 1)
            pool.memset(ones[:], 1.0).then_inc(consts_set, 1)
            pool.memset(zeros[:], 0.0).then_inc(consts_set, 1)
            pool.memset(lower[:], -4.0).then_inc(consts_set, 1)
            pool.memset(upper[:], 4.0).then_inc(consts_set, 1)
            pool.iota(number[:], pattern=[[0, 1]], base=1, channel_multiplier=1,
                      allow_small_or_imprecise_dtypes=True).then_inc(number_set, 1)
            pool.wait_ge(pool_step, 1)
            pool.affine_select(out=ident[:], in_=ident[:], compare_op=ALU.not_equal, fill=1.0, base=0,
                               pattern=[[-1, P]], channel_multiplier=1).then_inc(consts_set, 1)
            chain = 1
            for t in range(OT):
                sc = scale[:, t * GROUPS:(t + 1) * GROUPS].unsqueeze(2).broadcast_to([P, GROUPS, GSIZE])
                wg = w_q[:].rearrange("p (g n) -> p g n", g=GROUPS)
                pool.wait_ge(wq_diff, t + 1)
                pool.tensor_tensor(w_q[:], w_q[:], w_raw[:, t % 2], ALU.add).then_inc(pool_step, 1)
                chain += 1
                pool.wait_ge(pool_step, chain)
                pool.tensor_tensor(wg, wg, sc, ALU.mult).then_inc(pool_step, 1)
                chain += 1
                pool.wait_ge(pool_step, chain)
                pool.wait_ge(delta_copied, t + 1)
                if t:
                    pool.wait_ge(w_turned, t)
                pool.tensor_tensor(w_eff[:].rearrange("p c a i -> p a c i"),
                                   w_q[:].rearrange("p (a c i) -> p a c i", a=Q, c=C),
                                   delta[:, t % 2].rearrange("p (a c i) -> p a c i", a=Q, c=C),
                                   ALU.add).then_inc(pool_step, 1)
                chain += 1
                pool.wait_ge(pool_step, chain)
                a, c0 = t * P // KQ, t * P % KQ // 32
                dg = w_eff[:, c0:c0 + P // 32, a]
                pool.tensor_tensor(dg, dg, ident[:].rearrange("p (c i) -> p c i", i=32),
                                   ALU.add).then_inc(weff_made, 1)

        @block.vector
        def _(dve):
            steps = [0]

            def then(ins):
                steps[0] += 1
                ins.then_inc(step, 1)
                dve.wait_ge(step, steps[0])

            dve.wait_ge(sl_in, 16)
            then(dve.tensor_scalar(s_log[:], s_log[:], -120.0, 120.0, ALU.max, ALU.min))
            then(dve.tensor_scalar(s_k[:], s_log[:], LOG2E, ROUND, ALU.mult, ALU.add))
            then(dve.tensor_scalar(s_k[:], s_k[:], -ROUND, None, ALU.add))
            then(dve.scalar_tensor_tensor(s_log[:], s_k[:], -LN2_HI, s_log[:], ALU.mult, ALU.add))
            then(dve.scalar_tensor_tensor(s_log[:], s_k[:], -LN2_LO, s_log[:], ALU.mult, ALU.add))
            then(dve.tensor_scalar(s_k1[:], s_k[:], 0.5, ROUND, ALU.mult, ALU.add))
            then(dve.tensor_scalar(s_k1[:], s_k1[:], -ROUND, None, ALU.add))
            then(dve.tensor_tensor(s_k[:], s_k[:], s_k1[:], ALU.subtract))
            then(dve.tensor_scalar(s_p1[:], s_k1[:], 127.0, 8388608.0, ALU.add, ALU.mult))
            then(dve.tensor_scalar(s_p2[:], s_k[:], 127.0, 8388608.0, ALU.add, ALU.mult))
            then(dve.tensor_scalar(s_e[:], s_log[:], 1.0 / 5040, None, ALU.mult))
            for f in (720, 120, 24, 6, 2, 1):
                then(dve.scalar_tensor_tensor(s_e[:], s_e[:], 1.0 / f, s_log[:], ALU.add, ALU.mult))
            then(dve.tensor_scalar(s_e[:], s_e[:], 1.0, None, ALU.add))
            then(dve.tensor_tensor(s_e[:], s_e[:], s_p1[:].bitcast(F32), ALU.mult))
            then(dve.tensor_tensor(scale[:], s_e[:], s_p2[:].bitcast(F32), ALU.mult))
            then(dve.reciprocal(s_inv[:], scale[:]))

            dve.wait_ge(cb_in, 16)
            then(dve.tensor_reduce(cb_max[:, 0:1], cb[:], AX.X, ALU.max, apply_absolute_value=True))
            then(dve.tensor_scalar(cb_max[:, 0:1], cb_max[:, 0:1], 1e-8, None, ALU.max))
            then(dve.reciprocal(cb_max[:, 1:2], cb_max[:, 0:1]))
            then(dve.tensor_scalar(cb[:], cb[:], cb_max[:, 1:2], None, ALU.mult))
            then(dve.tensor_tensor(thr[:, 0:NCB - 1], cb[:, 0:NCB - 1], cb[:, 1:NCB], ALU.add))
            then(dve.tensor_scalar(thr[:, 0:NCB - 1], thr[:, 0:NCB - 1], 0.5, None, ALU.mult))

            dve.wait_ge(consts_set, 5)
            for level in range(LEVELS):
                half = NCB >> (level + 1)
                nodes = 1 << level

                def view(t):
                    return t[:].rearrange("p (n h e) -> p n h e", n=nodes, h=2)

                node = view(thr)[:, :, 0, half - 1:half].broadcast_to([P, nodes, half])
                then(dve.tensor_tensor(view(upper)[:, :, 0], view(upper)[:, :, 0], node, ALU.min))
                then(dve.tensor_tensor(view(lower)[:, :, 1], view(lower)[:, :, 1], node, ALU.max))

            then(dve.tensor_tensor(alive[:], lower[:], upper[:], ALU.is_lt))
            then(dve.tensor_tensor_scan(count[:], alive[:], zeros[:], 0.0, ALU.add, ALU.add))
            then(dve.tensor_tensor(alive[:], alive[:], count[:], ALU.mult))
            dve.wait_ge(number_set, 1)
            then(dve.scalar_tensor_tensor(junk[:, 0], alive[:], number[:], lower[:], ALU.is_equal, ALU.mult,
                                          accum_out=column[:, 0:1]))
            then(dve.scalar_tensor_tensor(junk[:, 1], alive[:], number[:], cb[:], ALU.is_equal, ALU.mult,
                                          accum_out=column[:, 1:2]))
            then(dve.tensor_scalar(column[:, 2:3], count[:, NCB - 1:NCB], number[:], NEVER, ALU.is_lt, ALU.mult))
            then(dve.tensor_tensor(column[:, 0:1], column[:, 0:1], column[:, 2:3], ALU.add))
            dve.tensor_scalar(diag[:, 0], ident[:], column[:, 0:1], None, ALU.mult).then_inc(diag_ready, 1)
            dve.tensor_scalar(diag[:, 1], ident[:], column[:, 1:2], None, ALU.mult).then_inc(diag_ready, 1)
            then(dve.tensor_scalar(trips[:], count[:, NCB - 1:NCB], -1.0, 1.0, ALU.add, ALU.max))
            dve.wait_ge(lists_made, 1)
            then(dve.tensor_copy(pieces[:].rearrange("p a n -> p (a n)"),
                                 p_delta[:, 0:2 * NCB]))
            turns = dve.value_load(trips[0:1, 0:1], min_val=1, max_val=MAX_PIECES - 1)
            dve.wait_ge(b_turned, 1)
            dve.tensor_scalar(b_t[:], p_turn[0:RANK].rearrange("p c n -> p (c n)"), LORA_SCALE, None, ALU.mult).then_inc(bt_ready, 1)

            def prepare_x(g, slot, g_val, sems_val):
                dve.wait_ge(x_in[slot % 2], sems_val)
                if g_val is not None:
                    dve.wait_ge(xhi_ready, g_val)
                    dve.wait_ge(xlo_ready, g_val)
                src = x_raw[:, slot % 2].rearrange("p b (c i) -> p b c i", i=32)
                dst = x_t[:].rearrange("p c (b j) -> p b c j", j=32)
                dve.transpose(dst, src).then_inc(xt_ready, 1)

            def split_x(slot, n_hi):
                dve.wait_ge(xhi_ready, n_hi)
                dve.tensor_tensor(x_lo[:, slot], x_t[:], x_hi[:, slot].bitcast(F32),
                                  ALU.subtract).then_inc(xlo_ready, 1)

            def lo_of_w(t):
                dve.wait_ge(whi_ready, t + 1)
                dve.tensor_tensor(w_lo[:, :, t * P:(t + 1) * P], p_turn[:],
                                  w_hi[:, :, t * P:(t + 1) * P].bitcast(F32), ALU.subtract).then_inc(wlo_ready, 1)

            def quantize(t):
                n = w_raw[:, t % 2]
                ng = n.rearrange("p (g n) -> p g n", g=GROUPS)
                si = s_inv[:, t * GROUPS:(t + 1) * GROUPS].unsqueeze(2).broadcast_to([P, GROUPS, GSIZE])
                dve.wait_ge(w_in[t % 2], 16 * (t // 2 + 1))
                dve.wait_ge(delta_made, t + 1)
                dve.tensor_tensor(n, n, p_delta[:], ALU.add).then_inc(delta_added, 1)
                dve.wait_ge(delta_added, t + 1)
                then(dve.tensor_tensor(ng, ng, si, ALU.mult))
                if t:
                    dve.wait_ge(weff_made, t)
                dve.tensor_copy(w_q[:], pieces[:, 1, 0:1].broadcast_to([P, I])).then_inc(piece_done, 1)
                with dve.Fori(0, turns) as j:
                    dve.wait_ge(piece_done, turns * (3 * t) + j * 3 + (t + 1))
                    dve.tensor_copy(value[:], pieces[:, 1, bass.ds(j + 1, 1)]).then_inc(piece_done, 1)
                    dve.tensor_scalar(mask[:], n, pieces[:, 0, bass.ds(j + 1, 1)], None,
                                      ALU.is_gt).then_inc(piece_done, 1)
                    dve.wait_ge(piece_done, turns * (3 * t) + j * 3 + (t + 3))
                    dve.nop(nofuse=True)
                    dve.copy_predicated(w_q[:], mask[:], value[:].broadcast_to([P, I])).then_inc(piece_done, 1)
                dve.wait_ge(piece_done, turns * (3 * t + 3) + (t + 1))
                dve.tensor_tensor(w_q[:], w_q[:], n, ALU.subtract).then_inc(wq_diff, 1)

            def resident_x(g):
                prepare_x(g, g, g if g else None, 64 * (g // 2 + 1))
                split_x(g, g + 1)

            resident_x(0)
            quantize(0)
            quantize(1)
            lo_of_w(0)
            resident_x(1)
            lo_of_w(1)
            for g in range(2, RES):
                resident_x(g)
            for t in range(2, OT):
                quantize(t)
                if t > 2:
                    lo_of_w(t - 1)
            lo_of_w(OT - 1)

            def group(n, r):
                g = (n + 1) * RES + r
                prepare_x(g, r, g, ((n + 1) * (RES // 2) + r // 2 + 1) * 64)
                dve.wait_ge(sums_done, UNITS + n * RT + 2 * r + 2 - RT)
                split_x(r, g + 1)

            with dve.Fori(0, NG // RES - 1) as n:
                for r in range(RES):
                    group(n, r)

        @block.scalar
        def _(act):
            act.dma_start(cb[:], cb_rows).then_inc(cb_in, 16)
            act.dma_start(s_log[:].rearrange("p (t g) -> p t g", t=OT), sl).then_inc(sl_in, 16)
            act.dma_start(b_sb[:], lb).then_inc(b_in, 16)
            act.dma_start(a_sb[:], lora_a).then_inc(a_in, 16)

            def hi_of_x(slot, n):
                act.wait_ge(xt_ready, n)
                act.copy(x_hi[:, slot], x_t[:]).then_inc(xhi_ready, 1)

            def copy_delta(t):
                act.wait_ge(delta_added, t + 1)
                if t >= 2:
                    act.wait_ge(weff_made, t - 1)
                act.copy(delta[:, t % 2], p_delta[:]).then_inc(delta_copied, 1)

            def hi_of_w(t):
                act.wait_ge(w_turned, t + 1)
                act.copy(w_hi[:, :, t * P:(t + 1) * P], p_turn[:]).then_inc(whi_ready, 1)

            def put_unit(u):
                act.wait_ge(sums_done, u + 1)
                if u >= 2:
                    act.wait_ge(y_gone[u % 2], 16 * (u // 2))
                act.copy(y_out[:, u % 2, 0:OB], acc_unit(u)).then_inc(y_ready, 1)

            def next_w(t):
                act.wait_ge(weff_made, t - 1)
                act.dma_start(w_raw[:, t % 2], wt[t]).then_inc(w_in[t % 2], 16)

            hi_of_x(0, 1)
            copy_delta(0)
            copy_delta(1)
            hi_of_w(0)
            next_w(2)
            hi_of_x(1, 2)
            hi_of_w(1)
            next_w(3)
            hi_of_x(2, 3)
            put_unit(0)
            hi_of_x(3, 4)
            put_unit(1)
            put_unit(2)
            copy_delta(2)
            for u in range(3, RT):
                put_unit(u)
            copy_delta(3)
            hi_of_w(2)
            next_w(4)
            copy_delta(4)
            hi_of_w(3)
            next_w(5)
            for b in range(1, NB - 1):
                t = 2 * b + 2
                copy_delta(t + 1)
                for u in range(RT):
                    put_unit(b * RT + u)
                    if u == 1:
                        hi_of_w(t)
                        if t + 2 < OT:
                            next_w(t + 2)
                    if u == 5 and t + 2 < OT:
                        copy_delta(t + 2)
                    if u == 6:
                        hi_of_w(t + 1)
                        if t + 3 < OT:
                            next_w(t + 3)
            for u in range(RT):
                if u in (2, 4):
                    act.wait_ge(sums_done, UNITS - RT + u)
                    hi_of_x(u // 2 - 1, RES + u // 2)
                put_unit(UNITS - RT + u)

            def turn(n, last):
                for r in range(RES):
                    if not (last and r >= RES - 2):
                        act.wait_ge(sums_done, UNITS - RT + n * RT + 2 * r + 6)
                        hi_of_x((r + 2) % RES, (n + 1) * RES + r + 3)
                    for h in range(2):
                        t = 2 * r + h
                        act.wait_ge(sums_done, UNITS + n * RT + t + 1)
                        act.wait_ge(y_gone[t % 2], 16 * (UNITS // 2) + n * (16 * RT // 2) + 16 * (t // 2))
                        act.copy(y_out[:, t % 2], acc[:, 2 * h:2 * h + 2].rearrange("p k n -> p (k n)")).then_inc(y_ready, 1)

            turns = NG // RES - 1
            with act.Fori(0, turns - 1) as n:
                turn(n, False)
            turn(turns - 1, True)

        @block.tensor
        def _(pe):
            pe.wait_ge(consts_set, 5)
            pe.wait_ge(b_in, 16)
            pb = p_turn[0:RANK].rearrange("p c n -> p (c n)")
            for t in range(OT):
                ins = pe.transpose(pb[:, t * P:(t + 1) * P], b_sb[:, t], ident[:])
            ins.then_inc(b_turned, 1)
            pe.wait_ge(diag_ready, 2)
            pe.matmul(p_delta[:, 0:2 * NCB], ones[:], diag[:].rearrange("p a n -> p (a n)"),
                      start=True, stop=True).then_inc(lists_made, 1)
            pe.wait_ge(bt_ready, 1)
            pe.wait_ge(a_in, 16)

            def make_delta(t):
                if t:
                    pe.wait_ge(delta_copied, t)
                for k in range(0, I, H):
                    ins = pe.matmul(p_delta[:, k:k + H], b_t[:, t * P:(t + 1) * P], a_sb[:, k:k + H],
                                    start=True, stop=True)
                ins.then_inc(delta_made, 1)

            def turn_w(t):
                pe.wait_ge(weff_made, t + 1)
                if t:
                    pe.wait_ge(wlo_ready, t)
                for c in range(C):
                    ins = pe.transpose(p_turn[:, c], w_eff[:, c].rearrange("p a i -> p (a i)"), ident[:])
                ins.then_inc(w_turned, 1)

            def passes(slot, half, cols):
                rows = slice(half * P, (half + 1) * P)
                for c in range(C):
                    for xs, ws in ((x_hi, (w_hi, w_lo)), (x_lo, (w_hi,))):
                        for w in ws:
                            for dst, col in cols:
                                yield (dst, xs[:, slot, c, rows], w[:, c, col],
                                       c == 0 and xs is x_hi and w is w_hi, c == C - 1 and xs is x_lo)

            def sum_up(slot, half, cols):
                for dst, xs, ws, first, last in passes(slot, half, cols):
                    ins = pe.matmul(dst, xs, ws, start=first, stop=last)
                ins.then_inc(sums_done, 1)

            make_delta(0)
            make_delta(1)
            turn_w(0)
            make_delta(2)
            turn_w(1)
            for b in range(NB):
                pe.wait_ge(wlo_ready, 2 * b + 2)
                for t in range(RT):
                    u = b * RT + t
                    if b == 0:
                        pe.wait_ge(xlo_ready, t // 2 + 1)
                    if u >= 4:
                        pe.wait_ge(y_ready, u - 3)
                    sum_up(t // 2, t % 2, [(acc_unit(u), slice(b * OB, (b + 1) * OB))])
                    if 0 < b < NB - 1:
                        if t == 1:
                            turn_w(2 * b + 2)
                            if 2 * b + 4 < OT:
                                make_delta(2 * b + 4)
                        if t == 6:
                            turn_w(2 * b + 3)
                        if t == 7 and 2 * b + 5 < OT:
                            make_delta(2 * b + 5)
                if b == 0:
                    make_delta(3)
                    turn_w(2)
                    make_delta(4)
                    turn_w(3)
                    make_delta(5)

            with pe.Fori(0, NG // RES - 1) as n:
                for t in range(RT):
                    if t % 2 == 0:
                        pe.wait_ge(xlo_ready, (n + 1) * RES + t // 2 + 1)
                    pe.wait_ge(y_ready, UNITS + n * RT + t - 1)
                    sum_up(t // 2, t % 2, [(acc[:, 2 * (t % 2) + k], slice(k * H, (k + 1) * H)) for k in range(2)])


_INS = ['x', 'condB_codebook', 'L0_cond_weight', 'L0_cond_scale_log', 'L0_cond_lora_A', 'L0_cond_lora_B']
_OUTS = [((128, 64, 1024), 'float32')]


def kernel(**inputs):
    import numpy as _np
    import concourse.bacc as _bacc
    from concourse import mybir as _mybir
    from concourse.bass_utils import run_bass_kernel_spmd as _run

    nc = _bacc.Bacc("TRN2", target_bir_lowering=False, num_devices=1)
    arrays, args = {}, []
    for name in _INS:
        a = _np.ascontiguousarray(inputs[name])
        arrays[f"in_{name}_dram"] = a
        args.append(nc.dram_tensor(f"in_{name}_dram", a.shape, _mybir.dt.from_np(a.dtype), kind="ExternalInput").ap())
    for i, (shape, dtype) in enumerate(_OUTS):
        dt = _mybir.dt.from_np(_np.dtype(dtype))
        args.append(nc.dram_tensor(f"out_{i}_dram", shape, dt, kind="ExternalOutput").ap())
    cond_residual_kernel(nc, *args)
    r = _run(nc, [arrays], core_ids=[0])
    got = tuple(r.results[0][f"out_{i}_dram"] for i in range(len(_OUTS)))
    return got[0]
```

```python
from contextlib import ExitStack

import concourse.bass as bass
from concourse import mybir

P = 128
ALU = mybir.AluOpType
ACT = mybir.ActivationFunctionType
AX = mybir.AxisListType
F32 = mybir.dt.float32
F32R = mybir.dt.float32r
I32 = mybir.dt.int32
U16 = mybir.dt.uint16
BF16 = mybir.dt.bfloat16

ROUND = 12582912.0
LOG2E = 1.4426950408889634
LN2_HI = 0.693145751953125
LN2_LO = 1.428606765330187e-06
NEVER = 3.0e38
LORA_SCALE = 32.0 / 64.0


def cond_residual_kernel(nc, x, codebook, weight, scale_log, lora_a, lora_b, out):
    I = x.shape[-1]
    O = weight.shape[0]
    ROWS = x.shape[0] * x.shape[1]
    RANK = lora_a.shape[0]
    NCB = codebook.shape[0]
    GROUPS = scale_log.shape[1]
    GSIZE = I // GROUPS
    C = I // P
    Q = P // 32
    KQ = I // Q
    OT = O // P
    TILES = ROWS // P
    GR = 2 * P
    NG = ROWS // GR
    RES = 4
    RT = RES * GR // P
    OB = 2 * P
    NB = O // OB
    H = 512
    LEVELS = NCB.bit_length() - 1
    assert 1 << LEVELS == NCB == P and I == O and NG % RES == 0

    xg = x.rearrange("s l k -> (s l) k").rearrange("(g b j) (a k) -> g a j b k", b=GR // 32, j=32, a=Q)
    og = out.rearrange("s l o -> (s l) o").rearrange("(t p) o -> t p o", p=P)
    wt = weight.rearrange("(t p) k -> t p k", p=P)
    sl = scale_log.rearrange("(t p) g one -> p t (g one)", p=P)
    lb = lora_b.rearrange("(t p) r -> p t r", p=P)
    cb_rows = codebook.partition_broadcast(P)

    with ExitStack() as ctx:
        def sb(name, shape, dt=F32):
            return ctx.enter_context(nc.sbuf_tensor(name, shape, dt))

        def ps(name, shape):
            return ctx.enter_context(nc.psum_tensor(name, shape, F32))

        def sem(name):
            return ctx.enter_context(nc.semaphore(name))

        w_hi = sb("w_hi", [P, C, O], F32R)
        w_lo = sb("w_lo", [P, C, O], F32R)
        x_hi = sb("x_hi", [P, RES, C, GR], F32R)
        x_lo = sb("x_lo", [P, RES, C, GR], F32R)
        x_raw = sb("x_raw", [P, 2, GR // 32, KQ])
        x_t = sb("x_t", [P, C, GR])
        y_out = sb("y_out", [P, 2, O])
        w_raw = sb("w_raw", [P, 2, I])
        w_q = sb("w_q", [P, 2, I])
        w_eff = sb("w_eff", [P, C, Q, 32])
        mask = sb("mask", [P, 2, I], BF16)
        delta = sb("delta", [P, 2, I])
        a_sb = sb("a_sb", [RANK, I])
        b_t = sb("b_t", [RANK, O])
        ident = sb("ident", [P, P])
        ones = sb("ones", [P, P])
        s_log = sb("s_log", [P, OT * GROUPS])
        s_k = sb("s_k", [P, OT * GROUPS])
        s_k1 = sb("s_k1", [P, OT * GROUPS])
        s_p1 = sb("s_p1", [P, OT * GROUPS], I32)
        s_p2 = sb("s_p2", [P, OT * GROUPS], I32)
        s_e = sb("s_e", [P, OT * GROUPS])
        scale = sb("scale", [P, OT * GROUPS])
        s_inv = sb("s_inv", [P, OT * GROUPS])
        tables = y_out[:].rearrange("p a n -> p (a n)")
        cb, thr, lower, upper, alive, zeros, count = (
            tables[:, i * NCB:(i + 1) * NCB] for i in range(7))
        junk = tables[:, 7 * NCB:9 * NCB].rearrange("p (a n) -> p a n", a=2)
        diag = tables[:, 9 * NCB:11 * NCB].rearrange("p (a n) -> p a n", a=2)
        b_sb = tables[:, 11 * NCB:11 * NCB + OT * RANK].rearrange("p (t r) -> p t r", t=OT)
        cb_max = sb("cb_max", [P, 2])
        number = sb("number", [P, 1])
        column = sb("column", [P, 3])
        pieces = sb("pieces", [P, 2, NCB])
        value = sb("value", [P, 2])
        half_count = sb("half_count", [P, 1])
        trips = sb("trips", [P, 1], I32)

        acc = ps("acc", [P, 4, H])
        p_delta = ps("p_delta", [P, I])
        p_turn = ps("p_turn", [P, C, P])

        x_in = [sem(f"x_in{i}") for i in range(2)]
        w_in = [sem(f"w_in{i}") for i in range(2)]
        y_gone = [sem(f"y_gone{i}") for i in range(2)]
        unit_gone = [sem(f"unit_gone{i}") for i in range(4)]
        cb_in = sem("cb_in")
        sl_in = sem("sl_in")
        a_in = sem("a_in")
        b_in = sem("b_in")
        consts_set = sem("consts_set")
        number_set = sem("number_set")
        step = sem("step")
        b_turned = sem("b_turned")
        bt_ready = sem("bt_ready")
        diag_ready = sem("diag_ready")
        lists_made = sem("lists_made")
        delta_made = sem("delta_made")
        delta_copied = sem("delta_copied")
        delta_added = sem("delta_added")
        pieces_ready = sem("pieces_ready")
        scale_ready = sem("scale_ready")
        normalized = sem("normalized")
        wq_set = sem("wq_set")
        mask_made = sem("mask_made")
        piece_done = sem("piece_done")
        picked = sem("picked")
        weff_made = sem("weff_made")
        pool_step = sem("pool_step")
        w_turned = sem("w_turned")
        whi_ready = sem("whi_ready")
        wlo_ready = sem("wlo_ready")
        xt_ready = sem("xt_ready")
        xhi_ready = sem("xhi_ready")
        xlo_ready = sem("xlo_ready")
        sums_done = sem("sums_done")
        y_ready = sem("y_ready")

        UNITS = NB * RT
        LATE = TILES - RT

        block = ctx.enter_context(nc.Block())

        def acc_unit(u):
            return acc[:, u % 4, 0:OB]

        def y_unit(u):
            return y_out[:, u % 4 // 2, u % 2 * H:u % 2 * H + OB]

        def finish_tile(eng, then, t):
            q, n = w_q[:, t % 2], w_raw[:, t % 2]
            sc = scale[:, t * GROUPS:(t + 1) * GROUPS].unsqueeze(2).broadcast_to([P, GROUPS, GSIZE])
            wg = q.rearrange("p (g n) -> p g n", g=GROUPS)
            then(eng.tensor_tensor(q, q, n, ALU.subtract))
            then(eng.tensor_tensor(q, q, n, ALU.add))
            then(eng.tensor_tensor(wg, wg, sc, ALU.mult))
            eng.wait_ge(delta_copied, t + 1)
            if t:
                eng.wait_ge(w_turned, t)
            then(eng.tensor_tensor(w_eff[:].rearrange("p c a i -> p a c i"),
                                   q.rearrange("p (a c i) -> p a c i", a=Q, c=C),
                                   delta[:, t % 2].rearrange("p (a c i) -> p a c i", a=Q, c=C), ALU.add))
            a, c0 = t * P // KQ, t * P % KQ // 32
            dg = w_eff[:, c0:c0 + P // 32, a]
            eng.tensor_tensor(dg, dg, ident[:].rearrange("p (c i) -> p c i", i=32),
                              ALU.add).then_inc(weff_made, 1)

        @block.sync
        def _(sp):
            def load_x(g, slot):
                for a in range(Q):
                    src = xg[g, a] if isinstance(g, int) else xg[bass.ds(g, 1), a].rearrange("g j b k -> (g j) b k")
                    sp.dma_start(x_raw[32 * a:32 * a + 32, slot], src).then_inc(x_in[slot], 16)

            def load_w(t):
                if t >= 2:
                    sp.wait_ge(weff_made, t - 1)
                sp.dma_start(w_raw[:, t % 2], wt[t]).then_inc(w_in[t % 2], 16)

            def next_x(g):
                sp.wait_ge(xt_ready, g - 1)
                load_x(g, g % 2)

            def store_units(first, last):
                for u in range(first, last):
                    sp.wait_ge(y_ready, u + 1)
                    t, b = u % RT, u // RT
                    sp.dma_start(og[t][:, b * OB:(b + 1) * OB], y_unit(u)).then_inc(unit_gone[u % 4], 16)

            load_w(0)
            load_x(0, 0)
            load_w(1)
            load_x(1, 1)
            next_x(2)
            load_w(2)
            next_x(3)
            load_w(3)
            next_x(4)
            load_w(4)
            next_x(5)
            for t in range(5, OT):
                store_units(4 * t - 20, 4 * t - 16)
                load_w(t)
            store_units(12, UNITS)

            def turn(n, last):
                for r in range(RES):
                    if not (last and r >= RES - 2):
                        sp.wait_ge(xt_ready, (n + 1) * RES + r + 1)
                        load_x((n + 1) * RES + r + 2, r % 2)
                    for h in range(2):
                        t = 2 * r + h
                        sp.wait_ge(y_ready, UNITS + n * RT + t + 1)
                        dst = og[(n + 1) * RT + t] if isinstance(n, int) else og[bass.ds((n + 1) * RT + t, 1)].rearrange("t p o -> (t p) o")
                        sp.dma_start(dst, y_out[:, t % 2]).then_inc(y_gone[t % 2], 16)

            turns = NG // RES - 1
            with sp.Fori(0, turns - 1) as n:
                turn(n, False)
            turn(turns - 1, True)
            for i in range(2):
                sp.wait_ge(y_gone[i], 16 * LATE // 2)

        @block.gpsimd
        def _(pool):
            pool.memset(ident[:], 0.0).then_inc(pool_step, 1)
            pool.memset(ones[:], 1.0).then_inc(consts_set, 1)
            pool.memset(zeros[:], 0.0).then_inc(consts_set, 1)
            pool.memset(lower[:], -4.0).then_inc(consts_set, 1)
            pool.memset(upper[:], 4.0).then_inc(consts_set, 1)
            pool.iota(number[:], pattern=[[0, 1]], base=1, channel_multiplier=1,
                      allow_small_or_imprecise_dtypes=True).then_inc(number_set, 1)
            pool.wait_ge(pool_step, 1)
            pool.affine_select(out=ident[:], in_=ident[:], compare_op=ALU.not_equal, fill=1.0, base=0,
                               pattern=[[-1, P]], channel_multiplier=1).then_inc(consts_set, 1)
            chain = 1

            def then(ins):
                nonlocal chain
                chain += 1
                ins.then_inc(pool_step, 1)
                pool.wait_ge(pool_step, chain)

            pool.wait_ge(sl_in, 16)
            then(pool.tensor_scalar(s_log[:], s_log[:], -120.0, 120.0, ALU.max, ALU.min))
            then(pool.tensor_scalar(s_k[:], s_log[:], LOG2E, ROUND, ALU.mult, ALU.add))
            then(pool.tensor_scalar(s_k[:], s_k[:], -ROUND, None, ALU.add))
            for part in (LN2_HI, LN2_LO):
                then(pool.tensor_scalar(s_e[:], s_k[:], -part, None, ALU.mult))
                then(pool.tensor_tensor(s_log[:], s_log[:], s_e[:], ALU.add))
            then(pool.tensor_scalar(s_k1[:], s_k[:], 0.5, ROUND, ALU.mult, ALU.add))
            then(pool.tensor_scalar(s_k1[:], s_k1[:], -ROUND, None, ALU.add))
            then(pool.tensor_tensor(s_k[:], s_k[:], s_k1[:], ALU.subtract))
            then(pool.tensor_scalar(s_p1[:], s_k1[:], 127.0, 8388608.0, ALU.add, ALU.mult))
            then(pool.tensor_scalar(s_p2[:], s_k[:], 127.0, 8388608.0, ALU.add, ALU.mult))
            then(pool.tensor_scalar(s_e[:], s_log[:], 1.0 / 5040, 1.0 / 720, ALU.mult, ALU.add))
            for f in (120, 24, 6, 2, 1, 1):
                then(pool.tensor_tensor(s_e[:], s_e[:], s_log[:], ALU.mult))
                then(pool.tensor_scalar(s_e[:], s_e[:], 1.0 / f, None, ALU.add))
            then(pool.tensor_tensor(s_e[:], s_e[:], s_p1[:].bitcast(F32), ALU.mult))
            pool.tensor_tensor(scale[:], s_e[:], s_p2[:].bitcast(F32), ALU.mult).then_inc(scale_ready, 1)
            pool.wait_ge(scale_ready, 1)

            def split_resident(g):
                pool.wait_ge(xhi_ready, g + 1)
                pool.tensor_tensor(x_lo[:, g], x_t[:], x_hi[:, g].bitcast(F32),
                                   ALU.subtract).then_inc(xlo_ready, 1)

            split_resident(0)
            for t in range(OT - 1):
                pool.wait_ge(picked, t + 1)
                finish_tile(pool, then, t)
                if t + 1 < RES:
                    split_resident(t + 1)

        @block.vector
        def _(dve):
            steps = [0]

            def then(ins):
                steps[0] += 1
                ins.then_inc(step, 1)
                dve.wait_ge(step, steps[0])

            def done(t, k):
                return pairs * (2 * t) + (t + k)

            def made(t, k):
                return pairs * (4 * t) + (2 * t + k)

            def prepare_x(g, slot, g_val, sems_val):
                dve.wait_ge(x_in[slot % 2], sems_val)
                if g_val is not None:
                    dve.wait_ge(xhi_ready, g_val)
                    dve.wait_ge(xlo_ready, g_val)
                src = x_raw[:, slot % 2].rearrange("p b (c i) -> p b c i", i=32)
                dst = x_t[:].rearrange("p c (b j) -> p b c j", j=32)
                dve.transpose(dst, src).then_inc(xt_ready, 1)

            dve.wait_ge(cb_in, 16)
            then(dve.tensor_reduce(cb_max[:, 0:1], cb[:], AX.X, ALU.max, apply_absolute_value=True))
            then(dve.tensor_scalar(cb_max[:, 0:1], cb_max[:, 0:1], 1e-8, None, ALU.max))
            then(dve.reciprocal(cb_max[:, 1:2], cb_max[:, 0:1]))
            then(dve.tensor_scalar(cb[:], cb[:], cb_max[:, 1:2], None, ALU.mult))
            then(dve.tensor_tensor(thr[:, 0:NCB - 1], cb[:, 0:NCB - 1], cb[:, 1:NCB], ALU.add))
            then(dve.tensor_scalar(thr[:, 0:NCB - 1], thr[:, 0:NCB - 1], 0.5, None, ALU.mult))

            dve.wait_ge(consts_set, 5)
            for level in range(LEVELS):
                half = NCB >> (level + 1)
                nodes = 1 << level

                def view(t):
                    return t.rearrange("p (n h e) -> p n h e", n=nodes, h=2)

                node = view(thr)[:, :, 0, half - 1:half].broadcast_to([P, nodes, half])
                then(dve.tensor_tensor(view(upper)[:, :, 0], view(upper)[:, :, 0], node, ALU.min))
                then(dve.tensor_tensor(view(lower)[:, :, 1], view(lower)[:, :, 1], node, ALU.max))

            then(dve.tensor_tensor(alive[:], lower[:], upper[:], ALU.is_lt))
            then(dve.tensor_tensor_scan(count[:], alive[:], zeros[:], 0.0, ALU.add, ALU.add))
            then(dve.tensor_tensor(alive[:], alive[:], count[:], ALU.mult))
            dve.wait_ge(number_set, 1)
            then(dve.scalar_tensor_tensor(junk[:, 0], alive[:], number[:], lower[:], ALU.is_equal, ALU.mult,
                                          accum_out=column[:, 0:1]))
            then(dve.scalar_tensor_tensor(junk[:, 1], alive[:], number[:], cb[:], ALU.is_equal, ALU.mult,
                                          accum_out=column[:, 1:2]))
            then(dve.tensor_scalar(column[:, 2:3], count[:, NCB - 1:NCB], number[:], NEVER, ALU.is_lt, ALU.mult))
            then(dve.scalar_tensor_tensor(column[:, 0:1], column[:, 0:1], -1.0, column[:, 2:3],
                                          ALU.mult, ALU.subtract))
            dve.tensor_scalar(diag[:, 0], ident[:], column[:, 0:1], None, ALU.mult).then_inc(diag_ready, 1)
            dve.tensor_scalar(diag[:, 1], ident[:], column[:, 1:2], None, ALU.mult).then_inc(diag_ready, 1)
            then(dve.tensor_scalar(half_count[:], count[:, NCB - 1:NCB], -2.0, 1.0, ALU.add, ALU.max))
            then(dve.tensor_scalar(half_count[:], half_count[:], 0.5, 0.25, ALU.mult, ALU.add))
            then(dve.tensor_scalar(half_count[:], half_count[:], ROUND, None, ALU.add))
            then(dve.tensor_scalar(trips[:], half_count[:], -ROUND, None, ALU.add))
            dve.wait_ge(lists_made, 1)
            dve.tensor_copy(pieces[:].rearrange("p a n -> p (a n)"),
                            p_delta[:, 0:2 * NCB]).then_inc(pieces_ready, 1)
            dve.wait_ge(b_turned, 1)
            dve.tensor_scalar(b_t[:], p_turn[0:RANK].rearrange("p c n -> p (c n)"), LORA_SCALE, None,
                              ALU.mult).then_inc(bt_ready, 1)
            prepare_x(0, 0, None, 64)
            dve.wait_ge(scale_ready, 1)
            dve.reciprocal(s_inv[:], scale[:]).then_inc(piece_done, 1)
            dve.wait_ge(pieces_ready, 1)
            dve.wait_ge(piece_done, 1)
            pairs = dve.value_load(trips[0:1, 0:1], min_val=1, max_val=NCB // 2 - 1)

            def split_x(slot, n_hi):
                dve.wait_ge(xhi_ready, n_hi)
                dve.tensor_tensor(x_lo[:, slot], x_t[:], x_hi[:, slot].bitcast(F32),
                                  ALU.subtract).then_inc(xlo_ready, 1)

            def lo_of_w(t):
                dve.wait_ge(whi_ready, t + 1)
                dve.tensor_tensor(w_lo[:, :, t * P:(t + 1) * P], p_turn[:],
                                  w_hi[:, :, t * P:(t + 1) * P].bitcast(F32), ALU.subtract).then_inc(wlo_ready, 1)

            def quantize(t):
                n = w_raw[:, t % 2]
                ng = n.rearrange("p (g n) -> p g n", g=GROUPS)
                si = s_inv[:, t * GROUPS:(t + 1) * GROUPS].unsqueeze(2).broadcast_to([P, GROUPS, GSIZE])
                dve.wait_ge(w_in[t % 2], 16 * (t // 2 + 1))
                dve.wait_ge(delta_made, t + 1)
                dve.tensor_tensor(n, n, p_delta[:], ALU.add).then_inc(delta_added, 1)
                dve.wait_ge(delta_added, t + 1)
                dve.tensor_tensor(ng, ng, si, ALU.mult).then_inc(normalized, 1)
                if t >= 2:
                    lo_of_w(t - 2)
                if 0 < t < RES:
                    prepare_x(t, t, t, 64 * (t // 2 + 1))
                q = w_q[:, t % 2]
                dve.wait_ge(wq_set, t + 1)
                dve.wait_ge(mask_made, made(t, 2))
                dve.nop(nofuse=True)
                dve.copy_predicated(q, mask[:, 1].bitcast(U16),
                                    value[:, 1:2].broadcast_to([P, I])).then_inc(piece_done, 1)
                with dve.Fori(0, pairs) as i:
                    for k in range(2):
                        dve.wait_ge(mask_made, made(t, i * 4 + (2 * k + 4)))
                        dve.nop(nofuse=True)
                        dve.wait_ge(piece_done, done(t, i * 2 + (k + 2)))
                        dve.nop(nofuse=True)
                        dve.copy_predicated(q, mask[:, k].bitcast(U16),
                                            value[:, k:k + 1].broadcast_to([P, I])).then_inc(piece_done, 1)
                dve.wait_ge(piece_done, done(t + 1, 1))
                dve.nop(nofuse=True).then_inc(picked, 1)
                if t == OT - 1:
                    dve.wait_ge(picked, OT)
                    finish_tile(dve, then, t)

            for t in range(OT):
                quantize(t)
            lo_of_w(OT - 2)
            lo_of_w(OT - 1)

            def group(n, r):
                g = (n + 1) * RES + r
                prepare_x(g, r, g, ((n + 1) * (RES // 2) + r // 2 + 1) * 64)
                dve.wait_ge(sums_done, UNITS + n * RT + 2 * r + 2 - RT)
                split_x(r, g + 1)

            with dve.Fori(0, NG // RES - 1) as n:
                for r in range(RES):
                    group(n, r)

        @block.scalar
        def _(act):
            act.dma_start(cb[:], cb_rows).then_inc(cb_in, 16)
            act.dma_start(s_log[:].rearrange("p (t g) -> p t g", t=OT), sl).then_inc(sl_in, 16)
            act.dma_start(b_sb, lb).then_inc(b_in, 16)
            act.dma_start(a_sb[:], lora_a).then_inc(a_in, 16)

            def hi_of_x(slot, n):
                act.wait_ge(xt_ready, n)
                act.copy(x_hi[:, slot], x_t[:]).then_inc(xhi_ready, 1)

            def copy_delta(t):
                act.wait_ge(delta_added, t + 1)
                if t >= 2:
                    act.wait_ge(weff_made, t - 1)
                act.copy(delta[:, t % 2], p_delta[:]).then_inc(delta_copied, 1)

            def hi_of_w(t):
                act.wait_ge(w_turned, t + 1)
                act.copy(w_hi[:, :, t * P:(t + 1) * P], p_turn[:]).then_inc(whi_ready, 1)

            def put_unit(u):
                act.wait_ge(sums_done, u + 1)
                if u >= 4:
                    act.wait_ge(unit_gone[u % 4], 16 * (u // 4))
                act.copy(y_unit(u), acc_unit(u)).then_inc(y_ready, 1)

            def start_q(t):
                if t >= 2:
                    act.wait_ge(weff_made, t - 1)
                act.copy(w_q[:, t % 2], pieces[:, 1, 0:1].broadcast_to([P, I])).then_inc(wq_set, 1)

            def masks(t):
                n = w_raw[:, t % 2]
                act.wait_ge(normalized, t + 1)
                if t:
                    act.wait_ge(piece_done, done(t, 1))
                act.copy(value[:, 1:2], pieces[:, 1, 1:2]).then_inc(mask_made, 1)
                act.activation(mask[:, 1], n, ACT.Relu, bias=pieces[:, 0, 1:2]).then_inc(mask_made, 1)
                if 0 < t < RES:
                    hi_of_x(t, t + 1)
                with act.Fori(0, pairs) as i:
                    for k in range(2):
                        act.wait_ge(piece_done, done(t, i * 2 + (k + 1)))
                        act.copy(value[:, k:k + 1], pieces[:, 1, bass.ds(i * 2 + (k + 2), 1)]).then_inc(mask_made, 1)
                        act.activation(mask[:, k], n, ACT.Relu,
                                       bias=pieces[:, 0, bass.ds(i * 2 + (k + 2), 1)]).then_inc(mask_made, 1)

            def done(t, k):
                return pairs * (2 * t) + (t + k)

            def put_units(first, last):
                for u in range(first, last):
                    put_unit(u)

            act.wait_ge(pieces_ready, 1)
            pairs = act.value_load(trips[0:1, 0:1], min_val=1, max_val=NCB // 2 - 1)
            hi_of_x(0, 1)
            for t in range(OT):
                start_q(t)
                copy_delta(t)
                masks(t)
                if t:
                    hi_of_w(t - 1)
                if t >= 3:
                    put_units(4 * t - 12, 4 * t - 8)
            hi_of_w(OT - 1)
            put_units(20, 24)
            for u in range(RT):
                if u in (2, 4):
                    act.wait_ge(sums_done, UNITS - RT + u)
                    hi_of_x(u // 2 - 1, RES + u // 2)
                put_unit(UNITS - RT + u)

            def turn(n, last):
                for r in range(RES):
                    if not (last and r >= RES - 2):
                        act.wait_ge(sums_done, UNITS - RT + n * RT + 2 * r + 6)
                        hi_of_x((r + 2) % RES, (n + 1) * RES + r + 3)
                    for h in range(2):
                        t = 2 * r + h
                        act.wait_ge(sums_done, UNITS + n * RT + t + 1)
                        if t >= 2:
                            act.wait_ge(y_gone[h], n * (16 * RT // 2) + 16 * r)
                        elif not isinstance(n, int) or n:
                            act.wait_ge(y_gone[h], n * (16 * RT // 2))
                        act.copy(y_out[:, t % 2], acc[:, 2 * h:2 * h + 2].rearrange("p k n -> p (k n)")).then_inc(y_ready, 1)

            for i in range(4):
                act.wait_ge(unit_gone[i], 16 * UNITS // 4)
            turns = NG // RES - 1
            turn(0, False)
            with act.Fori(1, turns - 1) as n:
                turn(n, False)
            turn(turns - 1, True)

        @block.tensor
        def _(pe):
            pe.wait_ge(consts_set, 5)
            pe.wait_ge(b_in, 16)
            pb = p_turn[0:RANK].rearrange("p c n -> p (c n)")
            for t in range(OT):
                ins = pe.transpose(pb[:, t * P:(t + 1) * P], b_sb[:, t], ident[:])
            ins.then_inc(b_turned, 1)
            pe.wait_ge(diag_ready, 2)
            pe.matmul(p_delta[:, 0:2 * NCB], ones[:], diag[:].rearrange("p a n -> p (a n)"),
                      start=True, stop=True).then_inc(lists_made, 1)
            pe.wait_ge(bt_ready, 1)
            pe.wait_ge(a_in, 16)

            def make_delta(t):
                if t:
                    pe.wait_ge(delta_copied, t)
                for k in range(0, I, H):
                    ins = pe.matmul(p_delta[:, k:k + H], b_t[:, t * P:(t + 1) * P], a_sb[:, k:k + H],
                                    start=True, stop=True)
                ins.then_inc(delta_made, 1)

            def turn_w(t):
                pe.wait_ge(weff_made, t + 1)
                if t:
                    pe.wait_ge(wlo_ready, t)
                for c in range(C):
                    ins = pe.transpose(p_turn[:, c], w_eff[:, c].rearrange("p a i -> p (a i)"), ident[:])
                ins.then_inc(w_turned, 1)

            def passes(slot, half, cols):
                rows = slice(half * P, (half + 1) * P)
                for c in range(C):
                    for xs, ws in ((x_hi, (w_hi, w_lo)), (x_lo, (w_hi,))):
                        for w in ws:
                            for dst, col in cols:
                                yield (dst, xs[:, slot, c, rows], w[:, c, col],
                                       c == 0 and xs is x_hi and w is w_hi, c == C - 1 and xs is x_lo)

            def sum_up(slot, half, cols):
                for dst, xs, ws, first, last in passes(slot, half, cols):
                    ins = pe.matmul(dst, xs, ws, start=first, stop=last)
                ins.then_inc(sums_done, 1)

            make_delta(0)
            make_delta(1)
            turn_w(0)
            make_delta(2)
            turn_w(1)
            make_delta(3)
            for b in range(NB):
                pe.wait_ge(wlo_ready, 2 * b + 2)
                for t in range(RT):
                    u = b * RT + t
                    if b == 0:
                        pe.wait_ge(xlo_ready, t // 2 + 1)
                    if u >= 4:
                        pe.wait_ge(y_ready, u - 3)
                    sum_up(t // 2, t % 2, [(acc_unit(u), slice(b * OB, (b + 1) * OB))])
                    if u % 4 == 0 and 4 + u // 4 < OT:
                        make_delta(4 + u // 4)
                    if u % 4 == 1 and 2 + u // 4 < OT:
                        turn_w(2 + u // 4)

            with pe.Fori(0, NG // RES - 1) as n:
                for t in range(RT):
                    if t % 2 == 0:
                        pe.wait_ge(xlo_ready, (n + 1) * RES + t // 2 + 1)
                    pe.wait_ge(y_ready, UNITS + n * RT + t - 1)
                    sum_up(t // 2, t % 2, [(acc[:, 2 * (t % 2) + k], slice(k * H, (k + 1) * H)) for k in range(2)])


_INS = ['x', 'condB_codebook', 'L0_cond_weight', 'L0_cond_scale_log', 'L0_cond_lora_A', 'L0_cond_lora_B']
_OUTS = [((128, 64, 1024), 'float32')]


def kernel(**inputs):
    import numpy as _np
    import concourse.bacc as _bacc
    from concourse import mybir as _mybir
    from concourse.bass_utils import run_bass_kernel_spmd as _run

    nc = _bacc.Bacc("TRN2", target_bir_lowering=False, num_devices=1)
    arrays, args = {}, []
    for name in _INS:
        a = _np.ascontiguousarray(inputs[name])
        arrays[f"in_{name}_dram"] = a
        args.append(nc.dram_tensor(f"in_{name}_dram", a.shape, _mybir.dt.from_np(a.dtype), kind="ExternalInput").ap())
    for i, (shape, dtype) in enumerate(_OUTS):
        dt = _mybir.dt.from_np(_np.dtype(dtype))
        args.append(nc.dram_tensor(f"out_{i}_dram", shape, dt, kind="ExternalOutput").ap())
    cond_residual_kernel(nc, *args)
    r = _run(nc, [arrays], core_ids=[0])
    got = tuple(r.results[0][f"out_{i}_dram"] for i in range(len(_OUTS)))
    return got[0]
```
